# Optimizing a Trainium2 kernel written in Bass

```python
import numpy as np
import jax
import jax.numpy as jnp

def _softmax(x, axis=-1):
    return jax.nn.softmax(x, axis=axis)

def _gelu(x):
    return jax.nn.gelu(x, approximate=True)

def _silu(x):
    return jax.nn.silu(x)

def _sigmoid(x):
    return jax.nn.sigmoid(x)

def _layernorm(x, axis=-1, eps=1e-05):
    m = jnp.mean(x, axis=axis, keepdims=True)
    v = jnp.var(x, axis=axis, keepdims=True)
    return (x - m) / jnp.sqrt(v + eps)

def _scatter_add(tgt, idx, src, axis=0):
    return tgt.at[idx].add(src)

def _segment_sum(src, seg, n):
    return jax.ops.segment_sum(src, seg, n)
kernel_name = 'mk_gnn_ffn_d1_gnn_r8_beac92'

def setup_inputs(seed: int=0):
    np.random.seed(seed)
    _w = jnp.asarray

    def _rec_inputs():
        import jax
        import jax.numpy as jnp
        _gk = jax.random.key(seed)
        x = -0.0001126 + 1 * jax.random.normal(jax.random.fold_in(_gk, 1), (1250, 768), jnp.float32)
        _s = jax.random.randint(jax.random.fold_in(_gk, 2), (20000,), 0, 1250, jnp.int32)
        _d = jax.random.randint(jax.random.fold_in(_gk, 3), (20000,), 0, 1250, jnp.int32)
        _loop = jnp.arange(1250, dtype=jnp.int32)
        src = jnp.concatenate([_s, _d, _loop])
        dst = jnp.concatenate([_d, _s, _loop])
        _o = jnp.argsort(dst, stable=True)
        src = src[_o]
        dst = dst[_o]
        return (x, src, dst)
    x, src, dst = _rec_inputs()

    def _L0_gnn_setup():
        import jax, jax.numpy as jnp
        import numpy as np
        N_NODES = 1250
        NEG_SLOPE = 0.2
        EPS = 1e-16

        def gat_layer(x, W, att_src, att_dst, bias, src, dst, heads, out_ch, concat):
            n = x.shape[0]
            h = (x @ W.T).reshape(n, heads, out_ch)
            a_src = jnp.einsum('nhc,hc->nh', h, att_src)
            a_dst = jnp.einsum('nhc,hc->nh', h, att_dst)
            e = a_src[src] + a_dst[dst]
            e = jax.nn.leaky_relu(e, NEG_SLOPE)
            m = jax.ops.segment_max(e, dst, num_segments=n)
            ex = jnp.exp(e - m[dst])
            denom = jax.ops.segment_sum(ex, dst, num_segments=n)
            alpha = ex / (denom[dst] + EPS)
            msg = alpha[:, :, None] * h[src]
            out = jax.ops.segment_sum(msg, dst, num_segments=n)
            if concat:
                out = out.reshape(n, heads * out_ch)
            else:
                out = out.mean(axis=1)
            return out + bias
        key = jax.random.key(seed)
        ks = jax.random.split(key, 12)
        x = jax.random.normal(ks[0], (N_NODES, 768), dtype=jnp.float32)
        edge_index = jax.random.randint(ks[1], (2, 20000), 0, N_NODES, dtype=jnp.int64)
        s1 = 1.0 / np.sqrt(768.0)
        W1 = jax.random.normal(ks[2], (8 * 128, 768), dtype=jnp.float32) * s1
        att_src1 = jax.random.normal(ks[3], (8, 128), dtype=jnp.float32) * (1.0 / np.sqrt(128.0))
        att_dst1 = jax.random.normal(ks[4], (8, 128), dtype=jnp.float32) * (1.0 / np.sqrt(128.0))
        b1 = jnp.zeros((8 * 128,), dtype=jnp.float32)
        s2 = 1.0 / np.sqrt(1024.0)
        W2 = jax.random.normal(ks[5], (1 * 768, 1024), dtype=jnp.float32) * s2
        att_src2 = jax.random.normal(ks[6], (1, 768), dtype=jnp.float32) * (1.0 / np.sqrt(768.0))
        att_dst2 = jax.random.normal(ks[7], (1, 768), dtype=jnp.float32) * (1.0 / np.sqrt(768.0))
        b2 = jnp.zeros((768,), dtype=jnp.float32)
        return {'x': x, 'edge_index': edge_index, 'W1': W1, 'att_src1': att_src1, 'att_dst1': att_dst1, 'b1': b1, 'W2': W2, 'att_src2': att_src2, 'att_dst2': att_dst2, 'b2': b2}
    _L0_gnn_all = _L0_gnn_setup()
    _L0_gnn_in = {k: v for k, v in _L0_gnn_all.items() if k in ('W1', 'att_src1', 'att_dst1', 'b1', 'W2', 'att_src2', 'att_dst2', 'b2')}
    del _L0_gnn_all

    def _L0_ffn_setup():
        import jax, jax.numpy as jnp
        import numpy as np
        key = jax.random.key(seed)
        ks = jax.random.split(key, 6)
        B, N, D, E, S, H = (4, 512, 768, 4, 1024, 384)
        sc = lambda d: 1.0 / np.sqrt(d)
        return {'x': jax.random.normal(ks[0], (B, N, D), dtype=jnp.float32), 'phi': jax.random.normal(ks[1], (E, S, D), dtype=jnp.float32) * sc(D), 'w1': jax.random.normal(ks[2], (E, D, H), dtype=jnp.float32) * sc(D), 'b1': jnp.zeros((E, H), dtype=jnp.float32), 'w2': jax.random.normal(ks[3], (E, H, D), dtype=jnp.float32) * sc(H), 'b2': jnp.zeros((E, D), dtype=jnp.float32)}
    _L0_ffn_all = _L0_ffn_setup()
    _L0_ffn_in = {k: v for k, v in _L0_ffn_all.items() if k in ('phi', 'w1', 'b1', 'w2', 'b2')}
    del _L0_ffn_all
    return {'x': x, 'src': src, 'dst': dst, 'L0_gnn_W1': _L0_gnn_in['W1'], 'L0_gnn_att_src1': _L0_gnn_in['att_src1'], 'L0_gnn_att_dst1': _L0_gnn_in['att_dst1'], 'L0_gnn_b1': _L0_gnn_in['b1'], 'L0_gnn_W2': _L0_gnn_in['W2'], 'L0_gnn_att_src2': _L0_gnn_in['att_src2'], 'L0_gnn_att_dst2': _L0_gnn_in['att_dst2'], 'L0_gnn_b2': _L0_gnn_in['b2'], 'L0_ffn_phi': _L0_ffn_in['phi'], 'L0_ffn_w1': _L0_ffn_in['w1'], 'L0_ffn_b1': _L0_ffn_in['b1'], 'L0_ffn_w2': _L0_ffn_in['w2'], 'L0_ffn_b2': _L0_ffn_in['b2']}

def reference(x, src, dst, L0_gnn_W1, L0_gnn_att_src1, L0_gnn_att_dst1, L0_gnn_b1, L0_gnn_W2, L0_gnn_att_src2, L0_gnn_att_dst2, L0_gnn_b2, L0_ffn_phi, L0_ffn_w1, L0_ffn_b1, L0_ffn_w2, L0_ffn_b2):
    import jax
    import jax.numpy as jnp

    def _L0_gnn_ref(x, edge_index, W1, att_src1, att_dst1, b1, W2, att_src2, att_dst2, b2):
        import jax, jax.numpy as jnp
        import numpy as np
        N_NODES = 1250
        NEG_SLOPE = 0.2
        EPS = 1e-16

        def gat_layer(x, W, att_src, att_dst, bias, src, dst, heads, out_ch, concat):
            n = x.shape[0]
            h = (x @ W.T).reshape(n, heads, out_ch)
            a_src = jnp.einsum('nhc,hc->nh', h, att_src)
            a_dst = jnp.einsum('nhc,hc->nh', h, att_dst)
            e = a_src[src] + a_dst[dst]
            e = jax.nn.leaky_relu(e, NEG_SLOPE)
            m = jax.ops.segment_max(e, dst, num_segments=n)
            ex = jnp.exp(e - m[dst])
            denom = jax.ops.segment_sum(ex, dst, num_segments=n)
            alpha = ex / (denom[dst] + EPS)
            msg = alpha[:, :, None] * h[src]
            out = jax.ops.segment_sum(msg, dst, num_segments=n)
            if concat:
                out = out.reshape(n, heads * out_ch)
            else:
                out = out.mean(axis=1)
            return out + bias
        src, dst = (edge_index[0], edge_index[1])
        h = gat_layer(x, W1, att_src1, att_dst1, b1, src, dst, heads=8, out_ch=128, concat=True)
        h = jax.nn.relu(h)
        out = gat_layer(h, W2, att_src2, att_dst2, b2, src, dst, heads=1, out_ch=768, concat=True)
        return out

    def _L0_ffn_ref(x, phi, w1, b1, w2, b2):
        import jax, jax.numpy as jnp
        import numpy as np
        logits = jnp.einsum('bnd,esd->bnes', x, phi)
        B, N, E, S = logits.shape
        dispatch = jax.nn.softmax(logits, axis=1)
        combine = jax.nn.softmax(logits.reshape(B, N, E * S), axis=-1).reshape(B, N, E, S)
        slots = jnp.einsum('bnd,bnes->besd', x, dispatch)
        h = jax.nn.gelu(jnp.einsum('besd,edh->besh', slots, w1) + b1[None, :, None, :])
        y = jnp.einsum('besh,ehd->besd', h, w2) + b2[None, :, None, :]
        out = jnp.einsum('besd,bnes->bnd', y, combine)
        return out
    edge_index = jnp.stack([src, dst])
    x = x + _L0_gnn_ref(_layernorm(x, axis=-1), edge_index, L0_gnn_W1, L0_gnn_att_src1, L0_gnn_att_dst1, L0_gnn_b1, L0_gnn_W2, L0_gnn_att_src2, L0_gnn_att_dst2, L0_gnn_b2)
    x = x + _L0_ffn_ref(_layernorm(x, axis=-1)[None], L0_ffn_phi, L0_ffn_w1, L0_ffn_b1, L0_ffn_w2, L0_ffn_b2)[0]
    return x

_drawn_inputs = setup_inputs


def setup_inputs(seed=0):
    import zlib

    import numpy as np

    out = dict(_drawn_inputs(seed))
    spreads = {'L0_gnn_b1': (0.0, 0.1),
     'L0_gnn_b2': (0.0, 0.1),
     'L0_ffn_b1': (0.0, 0.1),
     'L0_ffn_b2': (0.0, 0.1)}
    factors = {'L0_gnn_att_dst1': 8.0, 'L0_gnn_att_src2': 8.0, 'L0_gnn_att_dst2': 8.0}
    for name, (base, spread) in spreads.items():
        noise = np.random.default_rng([zlib.crc32(name.encode()), seed]).standard_normal(out[name].shape)
        drawn = base * np.exp(spread * noise) if base else spread * noise
        out[name] = jnp.asarray(drawn.astype(out[name].dtype))
    for name, factor in factors.items():
        out[name] = (out[name] * factor).astype(out[name].dtype)
    return out
```

```python
import numpy as np

import concourse.bass as bass
from concourse import mybir

F32 = mybir.dt.float32
F16 = mybir.dt.float16
I32 = mybir.dt.int32
ALU = mybir.AluOpType
ACT = mybir.ActivationFunctionType
AX_X = mybir.AxisListType.X
ds = bass.ds

P = 128
N = 1250
NT = -(-N // P)
NP = NT * P
E = 41250
BLOCK = 3
EB = -(-E // (P * BLOCK))
ET = EB * BLOCK
D = 768
KD = D // P
HEADS = 8
C1 = HEADS * P
KC = C1 // P
EXPERTS = 4
SLOTS = 1024
HID = 384
KH = HID // P
ST = EXPERTS * SLOTS // P
STE = SLOTS // P
HALF = N // 2
BANK = 512
CHUNKS = ((0, 512), (512, 512), (1024, N - 1024))
CHUNKS_PADDED = ((0, 512), (512, 512), (1024, NP - 1024))
NO_NODE = 4095
MASK = 1e30

S_NORM = 256.0
S_WEIGHT = 1024.0
S_ACT = 32.0
S_PROB = 4096.0
S_COMB = 1.0


def at_least(eng, sem, value):
    if not isinstance(value, int) or value > 0:
        eng.wait_ge(sem, value)


def split_product(eng, out, lhs, rhs, first, last):
    (lh, ll), (rh, rl) = lhs, rhs
    eng.matmul(out, lh, rh, start=first, stop=False, skip_group_check=True)
    eng.matmul(out, lh, rl, start=False, stop=False, skip_group_check=True)
    return eng.matmul(out, ll, rh, start=False, stop=last, skip_group_check=True)


def rolled(eng, step, first, loop_from, loop_to, end):
    assert (loop_to - loop_from) % 2 == 0
    for k in range(first, loop_from):
        step(k, k % 2)
    with eng.Fori(0, (loop_to - loop_from) // 2) as pair:
        for n in range(2):
            step(2 * pair + (loop_from + n), (loop_from + n) % 2)
    for k in range(loop_to, end):
        step(k, k % 2)


class Memory:

    def __init__(self, nc):
        self.nc, self.at = nc, -(-nc.sbuf_base // 64) * 64
        self.end, self.n = nc.sbuf_usable_end, 0

    def __call__(self, name, shape, dtype):
        size = int(np.prod(shape[1:])) * (2 if dtype == F16 else 4)
        assert self.at + size <= self.end, (name, self.at + size - self.end)
        self.n += 1
        got = self.nc.alloc_sbuf_tensor_at(f"{name}_{self.n}", list(shape), dtype, offset=self.at)
        self.at += -(-size // 64) * 64
        return got


def build(nc, x, edges, w1t, att1, gb1, w2t, att2, gb2, phi, fw1, fb1, fw2, fb2, out):
    mem = Memory(nc)

    taken = []

    def sem(name):
        taken.append(nc.alloc_semaphore(name=name))
        return taken[-1]

    def new_part():
        nc.all_engine_barrier()
        nc.clear_and_free_semaphores(taken)
        taken.clear()
        nc.all_engine_barrier()

    const = constants(nc, mem, sem)
    scratch = {
        "a1": nc.dram_tensor("a1_rows", [HEADS * NT, P], F32).ap(),
        "a2": nc.dram_tensor("a2_rows", [NT, P], F32).ap(),
        "row_max": nc.dram_tensor("row_max_rows", [NT, P], F32).ap(),
        "logits": nc.dram_tensor("logits_t", [ST, P, N], F32).ap(),
        "x1": nc.dram_tensor("x1", [NP, D], F32).ap(),
    }
    base = mem.at

    ln_c = mem("ln_c", [P, NT, NP], F32)
    h1t = [mem(f"h1t_{q}", [P, KC, NP], F16) for q in ("hi", "lo")]
    after_h1t = mem.at
    h = [mem(f"h_{q}", [P, NT, C1], F16) for q in ("hi", "lo")]
    nad1 = mem("nad1", [P, HEADS * NT], F32)
    temps = mem.at

    mem.at = after_h1t - 2 * KC * NP * 2 - NT * NP * 4
    xt = [mem(f"xt_{q}", [P, KD, NP], F16) for q in ("hi", "lo")]
    assert mem.at <= after_h1t
    mem.at = temps
    w1 = mem("w1", [P, KD, C1], F32)
    in_w1 = [sem(f"in_w1_{k}") for k in range(KD)]
    after_w1 = mem.at
    norm_and_turn(nc, mem, sem, const, "ln1", x, xt, w1, w1t.rearrange("(k p) c -> p k c", p=P),
                  in_w1)
    mem.at = after_w1
    node_products(nc, mem, sem, const, xt, w1, in_w1, att1, h, nad1, scratch["a1"])
    mem.at = temps
    count_edges(nc, mem, sem, const, edges, ln_c)
    mem.at = temps
    attend(nc, mem, sem, const, "gat1", HEADS, P, ln_c, h, nad1, scratch["a1"], gb1, turned=h1t)

    mem.at = after_h1t
    z = [mem(f"z_{q}", [P, NT, D], F16) for q in ("hi", "lo")]
    nad2 = mem("nad2", [P, NT], F32)
    temps = mem.at
    second_products(nc, mem, sem, const, h1t, w2t, att2, z, nad2, scratch["a2"])
    mem.at = temps
    attend(nc, mem, sem, const, "gat2", 1, D, ln_c, z, nad2, scratch["a2"], gb2,
           residual=x, stored=scratch["x1"])

    new_part()
    mem.at = base
    x2t = [mem(f"x2t_{q}", [P, KD, NP], F16) for q in ("hi", "lo")]
    xw_at = mem.at
    xw = [mem(f"xw_{q}", [P, NT, EXPERTS * HID], F16) for q in ("hi", "lo")]
    temps = mem.at
    ew1 = mem("ew1", [P, KD, EXPERTS * HID], F32)
    in_ew1 = [sem(f"in_ew1_{k}") for k in range(KD)]
    after_ew1 = mem.at
    mem.at = xw_at
    norm_and_turn(nc, mem, sem, const, "ln2", scratch["x1"], x2t, ew1, fw1, in_ew1)
    assert mem.at <= temps
    mem.at = after_ew1
    expert_inputs(nc, mem, sem, x2t, ew1, in_ew1, xw)
    mem.at = temps
    running_max = mem("running_max", [P, NP], F32)
    hid = [mem(f"hid_{q}", [P, ST, HID], F16) for q in ("hi", "lo")]
    end_hid = mem.at
    dispatch(nc, mem, sem, const, x2t, xw, phi, fb1, running_max, hid, scratch["logits"])
    mem.at = base
    comb = [mem(f"comb_{q}", [P, EXPERTS * KH, NP], F16) for q in ("hi", "lo")]
    end_comb = mem.at
    assert end_comb <= temps
    mem.at = end_hid
    slot_sums = mem("slot_sums", [EXPERTS, NP], F32)
    after_sums = mem.at
    mem.at = end_comb
    logits_in = mem("logits_in", [P, STE // 2, 2, HALF], F32)
    assert mem.at <= temps
    mem.at = after_sums
    combine(nc, mem, sem, const, running_max, hid, comb, slot_sums, logits_in,
            scratch["row_max"], scratch["logits"])
    mem.at = end_comb
    wf2 = mem("wf2", [P, EXPERTS * KH, D], F32)
    wt2 = [mem(f"wt2_{q}", [P, EXPERTS * KH, D], F16) for q in ("hi", "lo")]
    assert mem.at <= end_hid
    mem.at = after_sums
    expert_outputs(nc, mem, sem, comb, slot_sums, wf2, wt2, fw2, fb2, scratch["x1"], out)


def constants(nc, mem, sem):
    ident = mem("ident", [P, P], F32)
    picks = mem("picks", [P, EXPERTS, EXPERTS], F32)
    one = mem("one", [P, 1], F32)
    eps = mem("eps", [P, 1], F32)
    iota = mem("iota", [P, NP], F16)
    zeros = mem("zeros", [P, BANK], F16)
    filled, made = sem("const_filled"), sem("const_made")
    with nc.Block() as block:

        @block.gpsimd
        def _(eng):
            eng.memset(ident[:, :], 0.0).then_inc(filled, 1)
            eng.memset(picks[:, :, :], 0.0).then_inc(filled, 1)
            eng.memset(one[:, :], 1.0).then_inc(made, 1)
            eng.memset(eps[:, :], 1e-5).then_inc(made, 1)
            eng.memset(zeros[:, :], 0.0).then_inc(made, 1)
            eng.iota(iota[:, :], [[1, NP]], base=0, channel_multiplier=0,
                     allow_small_or_imprecise_dtypes=True).then_inc(made, 1)
            eng.wait_ge(filled, 2)
            eng.affine_select(out=ident[:, :], in_=ident[:, :], compare_op=ALU.not_equal, fill=1.0,
                              base=0, pattern=[[-1, P]], channel_multiplier=1).then_inc(made, 1)
            eng.affine_select(out=picks[:, :, :], in_=picks[:, :, :], compare_op=ALU.not_equal,
                              fill=1.0, base=0, pattern=[[1, EXPERTS], [-1, EXPERTS]],
                              channel_multiplier=0).then_inc(made, 1)
            eng.wait_ge(made, 6)

    return {"ident": ident, "picks": picks, "one": one, "eps": eps, "iota": iota, "zeros": zeros}


def norm_and_turn(nc, mem, sem, const, name, rows, turned, weights, stored_weights, in_weights):
    xs = mem("xs", [P, NT, D], F32)
    normed = mem("normed", [P, 2, D], F32)
    stats = mem("stats", [P, NT, 2, 6], F32)
    mv = mem("mv", [P, NT, 2], F32)
    dev = mem("dev", [P, NT], F32)
    rstd = mem("rstd", [P, NT], F32)
    loaded = [sem(f"{name}_loaded{t}") for t in range(NT)]
    stats_ready, mean_ready = sem(f"{name}_stats"), sem(f"{name}_mean")
    dev_ready, rstd_ready = sem(f"{name}_dev"), sem(f"{name}_rstd")
    normed_ready, turned_ready = sem(f"{name}_normed"), sem(f"{name}_turned")
    hi_ready, lo_ready = sem(f"{name}_hi"), sem(f"{name}_lo")
    hi, lo = turned
    with nc.psum_tensor(f"{name}_ps", [P, 2, 2 * BANK], F32) as ps, nc.Block() as block:

        @block.sync
        def _(eng):
            for t in range(NT):
                eng.dma_start(xs[:, t, :], rows[t * P:(t + 1) * P, :]).then_inc(loaded[t], 16)
            for k in range(KD):
                eng.dma_start(weights[:, k, :], stored_weights[:, k, :]).then_inc(in_weights[k], 16)

        @block.vector
        def _(eng):
            for t in range(NT):
                eng.wait_ge(loaded[t], 16)
                for c in range(2):
                    eng.bn_stats(stats[:, t, c, :], xs[:, t, c * (D // 2):(c + 1) * (D // 2)])\
                       .then_inc(stats_ready, 1)
            for t in range(NT):
                eng.wait_ge(stats_ready, 2 * NT)
                eng.bn_aggr(mv[:, t, :], stats[:, t, :, :]).then_inc(mean_ready, 1)
            eng.wait_ge(dev_ready, 1)
            eng.reciprocal(rstd[:, :], dev[:, :]).then_inc(rstd_ready, 1)
            eng.wait_ge(rstd_ready, 1)
            eng.tensor_scalar(rstd[:, :], rstd[:, :], S_NORM, None, ALU.mult).then_inc(rstd_ready, 1)
            eng.wait_ge(rstd_ready, 2)

            def low(t, u):
                eng.wait_ge(hi_ready, t + 1)
                eng.tensor_tensor(lo[:, :, ds(t * P, P)],
                                  ps[:, u, 0:D].rearrange("p (k n) -> p k n", k=KD),
                                  hi[:, :, ds(t * P, P)], ALU.subtract).then_inc(lo_ready, 1)

            def norm(t, u):
                eng.tensor_scalar(normed[:, u, :], xs[:, t, :], mv[:, t, 0:1], rstd[:, t:t + 1],
                                  ALU.subtract, ALU.mult).then_inc(normed_ready, 1)

            for t in range(NT):
                if t >= 2:
                    eng.wait_ge(turned_ready, t - 1)
                norm(t, t % 2)
                if t >= 1:
                    low(t - 1, (t - 1) % 2)
            low(NT - 1, (NT - 1) % 2)

        @block.scalar
        def _(eng):
            eng.wait_ge(mean_ready, NT)
            eng.activation(dev[:, :], mv[:, :, 1], ACT.Sqrt, bias=const["eps"][:, 0:1])\
               .then_inc(dev_ready, 1)
            for t in range(NT):
                eng.wait_ge(turned_ready, t + 1)
                eng.activation(hi[:, :, ds(t * P, P)],
                               ps[:, t % 2, 0:D].rearrange("p (k n) -> p k n", k=KD),
                               ACT.Copy).then_inc(hi_ready, 1)

        @block.tensor
        def _(eng):
            for t in range(NT):
                eng.wait_ge(normed_ready, t + 1)
                if t >= 2:
                    eng.wait_ge(lo_ready, t - 1)
                for k in range(KD):
                    last = eng.transpose(ps[:, t % 2, k * P:(k + 1) * P],
                                         normed[:, t % 2, k * P:(k + 1) * P], const["ident"][:, :])
                last.then_inc(turned_ready, 1)


def node_products(nc, mem, sem, const, xt, wf, in_wt, att1, h, nad, a_rows):
    wt = [mem(f"wt_{q}", [P, KD, C1], F16) for q in ("hi", "lo")]
    att = mem("att", [P, 2, C1], F32)
    weighted = mem("weighted", [P, 2, C1], F32)
    a_all = mem("a_all", [P, NT, 2 * HEADS], F32)
    a_src = mem("a_src", [P, HEADS, NT], F32)
    a_turned = mem("a_turned", [HEADS * NT, P], F32)
    in_att = sem("np_in_att")
    wt_hi, wt_lo = sem("np_wt_hi"), sem("np_wt_lo")
    h_done, h_hi, h_lo = sem("np_h"), sem("np_h_hi"), sem("np_h_lo")
    weighted_ready, a_done, a_read = sem("np_weighted"), sem("np_a"), sem("np_a_read")
    at_done, at_read, stored = sem("np_at"), sem("np_at_read"), sem("np_stored")
    to_act = S_ACT / (S_NORM * S_WEIGHT)
    with (
        nc.psum_tensor("np_h", [P, 2, 2 * BANK], F32) as hp,
        nc.psum_tensor("np_t", [P, BANK], F32) as tp,
        nc.Block() as block,
    ):
        @block.sync
        def _(eng):
            eng.dma_start(att[:, :, :], att1.unsqueeze(0).to_broadcast([P, 2, C1])).then_inc(in_att, 16)
            eng.wait_ge(at_read, 1)
            eng.dma_start(a_rows, a_turned[:, :]).then_inc(stored, 16)
            eng.wait_ge(stored, 16)

        @block.tensor
        def _(eng):
            def tile(t, u):
                at_least(eng, h_lo, t - 1)
                at_least(eng, weighted_ready, t - 1)
                for k in range(KD):
                    if isinstance(t, int) and t == 0:
                        eng.wait_ge(wt_lo, k + 1)
                    for c in range(2):
                        cols = slice(c * BANK, (c + 1) * BANK)
                        last = split_product(eng, hp[:, u, cols],
                                             [q[:, k, ds(t * P, P)] for q in xt],
                                             [q[:, k, cols] for q in wt], k == 0, k == KD - 1)
                last.then_inc(h_done, 1)

            tile(0, 0)
            tile(1, 1)
            with eng.Fori(1, NT // 2) as pair:
                for u in range(2):
                    tile(2 * pair + u, u)
            eng.wait_ge(a_read, 1)
            eng.transpose(tp[0:HEADS * NT, 0:P], a_src[:, :, :].rearrange("p h t -> p (h t)"),
                          const["ident"][:, :]).then_inc(at_done, 1)

        @block.scalar
        def _(eng):
            for k in range(KD):
                eng.wait_ge(in_wt[k], 16)
                eng.activation(wt[0][:, k, :], wf[:, k, :], ACT.Copy, scale=S_WEIGHT).then_inc(wt_hi, 1)
            with eng.Fori(0, NT // 2) as pair:
                for u in range(2):
                    t = 2 * pair + u
                    eng.wait_ge(h_done, t + 1)
                    eng.activation(h[0][:, ds(t, 1), :], hp[:, u, :], ACT.Copy, scale=to_act)\
                       .then_inc(h_hi, 1)
            eng.wait_ge(at_done, 1)
            eng.activation(a_turned[:, :], tp[0:HEADS * NT, 0:P], ACT.Copy).then_inc(at_read, 1)

        @block.vector
        def _(eng):
            for k in range(KD):
                eng.wait_ge(wt_hi, k + 1)
                eng.scalar_tensor_tensor(wt[1][:, k, :], wf[:, k, :], S_WEIGHT, wt[0][:, k, :],
                                         ALU.mult, ALU.subtract).then_inc(wt_lo, 1)
            eng.wait_ge(in_att, 16)
            for t in range(NT):
                eng.wait_ge(h_hi, t + 1)
                eng.scalar_tensor_tensor(h[1][:, t, :], hp[:, t % 2, :], to_act, h[0][:, t, :],
                                         ALU.mult, ALU.subtract).then_inc(h_lo, 1)
                if t >= 1:
                    eng.wait_ge(a_done, t)
                eng.tensor_tensor(weighted[:, :, :],
                                  hp[:, t % 2, :].unsqueeze(1).to_broadcast([P, 2, C1]),
                                  att[:, :, :], ALU.mult).then_inc(weighted_ready, 1)
                eng.wait_ge(weighted_ready, t + 1)
                eng.tensor_reduce(a_all[:, t, :], weighted[:, :, :].rearrange("p s (h c) -> p (s h) c", c=P),
                                  AX_X, ALU.add).then_inc(a_done, 1)
            eng.wait_ge(a_done, NT)
            un = 1.0 / (S_NORM * S_WEIGHT)
            eng.tensor_scalar(a_src[:, :, :], a_all[:, :, 0:HEADS].rearrange("p t h -> p h t"),
                              un, None, ALU.mult).then_inc(a_read, 1)
            eng.tensor_scalar(nad[:, :].rearrange("p (h t) -> p h t", h=HEADS),
                              a_all[:, :, HEADS:].rearrange("p t h -> p h t"),
                              -0.8 * un, None, ALU.mult).then_inc(a_read, 1)
            eng.wait_ge(a_read, 2)


def count_edges(nc, mem, sem, const, edges, ln_c):
    RING = 3
    raw = mem("raw", [P, 2, ET], I32)
    src = mem("src", [P, ET], F32)
    dst = mem("dst", [P, ET], F32)
    dst_tile_i = mem("dst_tile_i", [P, ET], I32)
    dst_tile = mem("dst_tile", [P, ET], F16)
    up = mem("up", [P, ET], F16)
    down = mem("down", [P, ET], F16)
    tiles = mem("tiles", [P, NT], F16)
    reused = mem.at
    within = mem("within", [P, NT, ET], F16)
    ranks = mem("ranks", [P, NT, ET], F16)
    free_again = mem.at
    mem.at = reused
    counted = mem("counted", [P, 2, NP], F32)
    lns = mem("lns", [P, NP], F32)
    penalty = mem("penalty", [P, NP], F32)
    mem.at = max(mem.at, free_again)
    ends = mem("ends", [P, 2 * NT], F32)
    top = mem("top", [2 * NT, 1], F32)
    row = mem("row", [1, 8, NT], F32)
    bounds = mem("bounds", [1, 3, NT], I32)
    one_src = mem("one_src", [P, RING * BLOCK, NP], F16)
    one_dst = mem("one_dst", [P, RING * BLOCK, P], F16)
    loaded, iotas, casts, prep = sem("ce_loaded"), sem("ce_iotas"), sem("ce_casts"), sem("ce_prep")
    ends_turned, top_ready, top_turned = sem("ce_ends_t"), sem("ce_top"), sem("ce_top_t")
    rows, bounds_ready = sem("ce_rows"), sem("ce_bounds")
    src_ready, dst_ready, free = sem("ce_src"), sem("ce_dst"), sem("ce_free")
    count_done, atleast1, ln_ready = sem("ce_count"), sem("ce_atleast1"), sem("ce_ln")
    pen_ready, out_ready = sem("ce_pen"), sem("ce_out")
    with (
        nc.psum_tensor("ce_c", [P, 2, 3 * BANK], F32) as cp,
        nc.psum_tensor("ce_t", [P, BANK], F32) as tp,
        nc.Block() as block,
    ):

        @block.sync
        def _(eng):
            eng.dma_start(raw[:, :, :], edges).then_inc(loaded, 16)

        def spans(eng):
            eng.wait_ge(bounds_ready, 3)
            for j in range(NT):
                first = eng.value_load(bounds[0:1, 0, j:j + 1], min_val=0, max_val=NT * EB - 1)
                last = eng.value_load(bounds[0:1, 1, j:j + 1], min_val=1, max_val=NT * EB)
                shift = eng.value_load(bounds[0:1, 2, j:j + 1], min_val=-NT * EB, max_val=EB)
                yield j, first, last, shift

        def edge_block(k, shift):
            return nc.s_assert_within(k + shift, 0, EB - 1, skip_runtime_bounds_check_because=(
                "the bounds are clamped to the blocks of edges"))

        @block.gpsimd
        def _(eng):
            eng.iota(up[:, :], [[1, EB], [0, BLOCK]], base=1, channel_multiplier=0,
                     allow_small_or_imprecise_dtypes=True).then_inc(iotas, 1)
            eng.iota(down[:, :], [[-1, EB], [0, BLOCK]], base=EB, channel_multiplier=0,
                     allow_small_or_imprecise_dtypes=True).then_inc(iotas, 1)
            eng.iota(tiles[:, :], [[1, NT]], base=0, channel_multiplier=0,
                     allow_small_or_imprecise_dtypes=True).then_inc(iotas, 1)
            eng.wait_ge(iotas, 3)

        @block.vector
        def _(eng):
            eng.wait_ge(loaded, 16)
            eng.tensor_copy(src[:, :], raw[:, 0, :]).then_inc(casts, 1)
            eng.tensor_copy(dst[:, :], raw[:, 1, :]).then_inc(casts, 1)
            eng.tensor_scalar(dst_tile_i[:, :], raw[:, 1, :], P.bit_length() - 1, None,
                              ALU.arith_shift_right).then_inc(casts, 1)
            eng.wait_ge(casts, 3)
            eng.tensor_copy(dst_tile[:, :], dst_tile_i[:, :]).then_inc(casts, 1)
            eng.wait_ge(casts, 4)
            eng.wait_ge(iotas, 3)
            full = [P, NT, ET]
            eng.tensor_tensor(within[:, :, :], dst_tile[:, :].unsqueeze(1).to_broadcast(full),
                              tiles[:, :].unsqueeze(2).to_broadcast(full), ALU.is_equal).then_inc(prep, 1)
            for n, rank in enumerate((up, down)):
                eng.wait_ge(prep, 2 * n + 1)
                eng.tensor_tensor(ranks[:, :, :], within[:, :, :],
                                  rank[:, :].unsqueeze(1).to_broadcast(full), ALU.mult).then_inc(prep, 1)
                eng.wait_ge(prep, 2 * n + 2)
                eng.tensor_reduce(ends[:, n * NT:(n + 1) * NT], ranks[:, :, :], AX_X, ALU.max)\
                   .then_inc(prep, 1)
            eng.wait_ge(prep, 5)
            eng.wait_ge(ends_turned, 1)
            eng.tensor_reduce(top[:, :], tp[0:2 * NT, 0:P], AX_X, ALU.max).then_inc(top_ready, 1)
            eng.wait_ge(top_turned, 1)
            r = row
            eng.tensor_scalar(r[:, 0, :], tp[0:1, P + NT:P + 2 * NT], -1.0, float(EB),
                              ALU.mult, ALU.add).then_inc(rows, 1)
            eng.wait_ge(rows, 1)
            eng.tensor_scalar(r[:, 0, :], r[:, 0, :], float(EB - 1), None, ALU.min)\
               .then_inc(rows, 1)
            eng.wait_ge(rows, 2)
            eng.tensor_scalar(r[:, 1, :], r[:, 0, :], 1.0, None, ALU.add).then_inc(rows, 1)
            eng.wait_ge(rows, 3)
            eng.tensor_tensor(r[:, 1, :], r[:, 1, :], tp[0:1, P:P + NT], ALU.max).then_inc(rows, 1)
            eng.wait_ge(rows, 4)
            eng.tensor_tensor(r[:, 2, :], r[:, 1, :], r[:, 0, :], ALU.subtract).then_inc(rows, 1)
            eng.memset(r[:, 3, :], 1.0).then_inc(rows, 1)
            eng.wait_ge(rows, 6)
            eng.tensor_tensor_scan(r[:, 4, :], r[:, 3, :], r[:, 2, :], 0.0, ALU.mult, ALU.add)\
               .then_inc(rows, 1)
            eng.wait_ge(rows, 7)
            eng.tensor_tensor(r[:, 5, :], r[:, 4, :], r[:, 2, :], ALU.subtract).then_inc(rows, 1)
            eng.wait_ge(rows, 8)
            eng.tensor_tensor(r[:, 6, :], r[:, 0, :], r[:, 5, :], ALU.subtract).then_inc(rows, 1)
            eng.wait_ge(rows, 9)
            for n, q in enumerate((5, 4, 6)):
                eng.tensor_copy(bounds[:, n, :], row[:, q, :]).then_inc(bounds_ready, 1)

            def finish(j):
                eng.wait_ge(count_done, j + 1)
                c = cp[:, j % 2, 0:NP]
                if j >= 1:
                    eng.wait_ge(ln_ready, j)
                eng.tensor_scalar(counted[:, j % 2, :], c, 1.0, None, ALU.max).then_inc(atleast1, 1)
                if j >= 1:
                    eng.wait_ge(out_ready, j)
                eng.tensor_scalar(penalty[:, :], c, 1.0, 1.0, ALU.min, ALU.subtract)\
                   .then_inc(pen_ready, 1)
                eng.wait_ge(pen_ready, j + 1)
                eng.wait_ge(ln_ready, j + 1)
                eng.scalar_tensor_tensor(ln_c[:, j, :], penalty[:, :], MASK, lns[:, :],
                                         ALU.mult, ALU.add).then_inc(out_ready, 1)

            for j, first, last, shift in spans(eng):
                with eng.Fori(first, last) as k:
                    eng.wait_ge(free, k + 1)
                    block_at = edge_block(k, shift) * BLOCK
                    slot = (k % RING) * BLOCK
                    for i in range(BLOCK):
                        eng.tensor_scalar(one_src[:, ds(slot + i, 1), :], const["iota"][:, :],
                                          src[:, ds(block_at + i, 1)], None, ALU.is_equal)\
                           .then_inc(src_ready, 1)
                    eng.tensor_tensor(one_dst[:, ds(slot, BLOCK), :],
                                      const["iota"][:, j * P:(j + 1) * P].unsqueeze(1)
                                      .to_broadcast([P, BLOCK, P]),
                                      dst[:, ds(block_at, BLOCK)].unsqueeze(2)
                                      .to_broadcast([P, BLOCK, P]), ALU.is_equal)\
                       .then_inc(dst_ready, 1)
                if j >= 1:
                    finish(j - 1)
            finish(NT - 1)
            eng.wait_ge(out_ready, NT)

        @block.scalar
        def _(eng):
            for j in range(NT):
                eng.wait_ge(atleast1, j + 1)
                if j >= 1:
                    eng.wait_ge(out_ready, j)
                eng.activation(lns[:, :], counted[:, j % 2, :], ACT.Ln).then_inc(ln_ready, 1)

        @block.tensor
        def _(eng):
            zeros = const["zeros"]
            eng.wait_ge(prep, 5)
            eng.transpose(tp[0:2 * NT, 0:P], ends[:, :], const["ident"][:, :]).then_inc(ends_turned, 1)
            eng.wait_ge(top_ready, 1)
            eng.transpose(tp[0:1, P:P + 2 * NT], top[:, :], const["ident"][0:2 * NT, 0:2 * NT])\
               .then_inc(top_turned, 1)
            eng.matmul(cp[:, 0, 0:P], zeros[:, 0:P], zeros[:, 0:P], start=True, stop=True)\
               .then_inc(free, RING)
            for j, first, last, shift in spans(eng):
                if j >= 2:
                    eng.wait_ge(out_ready, j - 1)
                for a, n in CHUNKS_PADDED:
                    eng.matmul(cp[:, j % 2, a:a + n], zeros[:, 0:P], zeros[:, 0:n],
                               start=True, stop=False, skip_group_check=True)
                with eng.Fori(first, last) as k:
                    eng.wait_ge(src_ready, k * BLOCK + BLOCK)
                    eng.wait_ge(dst_ready, k + 1)
                    slot = (k % RING) * BLOCK
                    for i in range(BLOCK):
                        for a, n in CHUNKS_PADDED:
                            mm = eng.matmul(cp[:, j % 2, a:a + n], one_dst[:, ds(slot + i, 1), :],
                                            one_src[:, ds(slot + i, 1), a:a + n],
                                            start=False, stop=False, skip_group_check=True)
                    mm.then_inc(free, 1)
                for a, n in CHUNKS_PADDED:
                    mm = eng.matmul(cp[:, j % 2, a:a + n], zeros[:, 0:P], zeros[:, 0:n],
                                    start=False, stop=True, skip_group_check=True)
                mm.then_inc(count_done, 1)


def attend(nc, mem, sem, const, name, heads, width, ln_c, h, nad, a_rows, bias, turned=None,
           residual=None, stored=None):
    steps = heads * NT
    s_row = mem("s_row", [P, 2, NP], F32)
    relus = mem("relus", [P, 2, NP], F32)
    base = mem("base", [P, 2, NP], F32)
    q = mem("q", [P, 2, NP], F32)
    pt = [mem(f"pt_{x}", [P, 2, NT, P], F16) for x in ("hi", "lo")]
    top = mem("top", [P, 2], F32)
    neg_top = mem("neg_top", [P, 2], F32)
    gate = mem("gate", [P, 2], F32)
    some_edge = mem("some_edge", [P, 4], F32)
    den = mem("den", [P, 4], F32)
    inv = mem("inv", [P, 2], F32)
    factor = mem("factor", [P, 2], F32)
    rows = mem("rows", [P, 2, width], F32)
    bias_all = mem("bias_all", [P, heads * width], F32)
    in_bias, bias_ready = sem(f"{name}_in_bias"), sem(f"{name}_bias")
    in_s = sem(f"{name}_in_s")
    relu_ready, base_ready, q_ready = sem(f"{name}_relu"), sem(f"{name}_base"), sem(f"{name}_q")
    edge_ready, neg_ready, p_ready = sem(f"{name}_edge"), sem(f"{name}_neg"), sem(f"{name}_p")
    pt_turned, hi_ready, lo_ready = sem(f"{name}_ptt"), sem(f"{name}_hi"), sem(f"{name}_lo")
    out_done, inv_ready, factor_ready = sem(f"{name}_out"), sem(f"{name}_inv"), sem(f"{name}_factor")
    rows_ready, rows_turned = sem(f"{name}_rows"), sem(f"{name}_rows_t")
    th_ready, tl_ready = sem(f"{name}_th"), sem(f"{name}_tl")
    in_x, sum_ready, saved = [sem(f"{name}_in_x{i}") for i in range(2)], sem(f"{name}_sum"), [
        sem(f"{name}_saved{i}") for i in range(2)]
    xs = mem("res", [P, 2, width], F32) if residual is not None else None
    out_scale = S_ACT if turned else 1.0

    with (
        nc.psum_tensor(f"{name}_pt", [P, 2, 3 * BANK], F32) as tp,
        nc.psum_tensor(f"{name}_o", [P, 2, BANK], F32) as op,
        nc.Block() as block,
    ):

        def run(eng, step):
            rolled(eng, step, -1, 5, steps - 1, steps + 3)

        def valid(k):
            return not isinstance(k, int) or 0 <= k < steps

        def head_tile(k):
            return k // NT, k % NT

        @block.sync
        def _(eng):
            eng.dma_start(bias_all[:, :], bias.to_broadcast([P, heads * width])).then_inc(in_bias, 16)

            def load_s(head, slot):
                at_least(eng, in_s, 16 * head)
                at_least(eng, relu_ready, (head - 1) * NT)
                at_least(eng, base_ready, (head - 1) * NT)
                eng.dma_start(s_row[:, slot, :].rearrange("p (t n) -> p t n", t=NT),
                              a_rows[ds(head * NT, NT), :].unsqueeze(0).to_broadcast([P, NT, P]))\
                   .then_inc(in_s, 16)

            for head in range(min(heads, 2)):
                load_s(head, head)
            if heads > 2:
                with eng.Fori(1, heads // 2) as pair:
                    for slot in range(2):
                        load_s(2 * pair + slot, slot)
            if residual is not None:
                def load_x(k):
                    eng.dma_start(xs[:, k % 2, :], residual[k * P:(k + 1) * P, :])\
                       .then_inc(in_x[k % 2], 16)

                load_x(0)
                load_x(1)
                for k in range(steps):
                    eng.wait_ge(rows_ready, k + 1)
                    eng.dma_start(stored[k * P:(k + 1) * P, :], rows[:, k % 2, :])\
                       .then_inc(saved[k % 2], 16)
                    if k + 2 < steps:
                        load_x(k + 2)
                for u in range(2):
                    eng.wait_ge(saved[u], 16 * (steps // 2))

        @block.gpsimd
        def _(eng):
            def step(k, u):
                if valid(k + 1):
                    w = (u + 1) % 2
                    head, j = head_tile(k + 1)
                    eng.wait_ge(in_s, 16 * (head + 1))
                    at_least(eng, q_ready, k)
                    eng.tensor_tensor(base[:, w, :], s_row[:, ds(head % 2, 1), :],
                                      ln_c[:, ds(j, 1), :], ALU.add).then_inc(base_ready, 1)
            run(eng, step)

        @block.scalar
        def _(eng):
            eng.wait_ge(in_bias, 16)
            eng.activation(bias_all[:, :], bias_all[:, :], ACT.Copy, scale=out_scale)\
               .then_inc(bias_ready, 1)

            def step(k, u):
                w = (u + 1) % 2
                if valid(k + 1):
                    head, j = head_tile(k + 1)
                    eng.wait_ge(in_s, 16 * (head + 1))
                    at_least(eng, q_ready, k)
                    eng.activation(relus[:, w, :], s_row[:, ds(head % 2, 1), :], ACT.Relu,
                                   bias=nad[:, ds(k + 1, 1)], scale=-0.8).then_inc(relu_ready, 1)
                if valid(k):
                    eng.wait_ge(neg_ready, k + 1)
                    at_least(eng, factor_ready, k - 1)
                    eng.activation(q[:, u, :], q[:, u, :], ACT.Exp, bias=neg_top[:, u:u + 1],
                                   accum_out=den[:, u:u + 1]).then_inc(p_ready, 1)
                if turned and valid(k - 3):
                    head, j = head_tile(k - 3)
                    eng.wait_ge(rows_turned, k - 2)
                    eng.activation(turned[0][:, ds(head, 1), ds(j * P, P)],
                                   op[:, w, P:2 * P], ACT.Relu).then_inc(th_ready, 1)
                if valid(k - 1):
                    eng.wait_ge(pt_turned, k)
                    at_least(eng, out_done, k - 2)
                    eng.activation(pt[0][:, w, :, :].rearrange("p t n -> p (t n)"),
                                   tp[:, w, 0:NP], ACT.Copy, scale=S_PROB).then_inc(hi_ready, 1)
            run(eng, step)

        @block.vector
        def _(eng):
            eng.wait_ge(bias_ready, 1)

            def step(k, u):
                w = (u + 1) % 2
                if valid(k + 1):
                    eng.wait_ge(relu_ready, k + 2)
                    eng.wait_ge(base_ready, k + 2)
                    at_least(eng, edge_ready, k)
                    at_least(eng, pt_turned, k)
                    eng.memset(gate[:, w:w + 1], 0.0)
                    eng.tensor_tensor_reduce(q[:, w, :], relus[:, w, :], base[:, w, :], 1.0, -3e38,
                                             ALU.add, ALU.max, top[:, w:w + 1]).then_inc(q_ready, 1)
                    eng.wait_ge(q_ready, k + 2)
                    at_least(eng, p_ready, k)
                    eng.tensor_scalar(neg_top[:, w:w + 1], top[:, w:w + 1], -1.0, None, ALU.mult)\
                       .then_inc(neg_ready, 1)
                    at_least(eng, factor_ready, k)
                    eng.tensor_scalar(some_edge[:, w:w + 1], top[:, w:w + 1], -MASK / 2,
                                      1.0 / (S_PROB * S_ACT) * out_scale, ALU.is_gt, ALU.mult)\
                       .then_inc(edge_ready, 1)
                if turned and valid(k - 3):
                    head, j = head_tile(k - 3)
                    eng.wait_ge(th_ready, k - 2)
                    eng.scalar_tensor_tensor(turned[1][:, ds(head, 1), ds(j * P, P)],
                                             op[:, w, P:2 * P], 0.0,
                                             turned[0][:, ds(head, 1), ds(j * P, P)],
                                             ALU.max, ALU.subtract).then_inc(tl_ready, 1)
                if valid(k - 1):
                    eng.wait_ge(hi_ready, k)
                    eng.scalar_tensor_tensor(pt[1][:, w, :, :].rearrange("p t n -> p (t n)"),
                                             tp[:, w, 0:NP], S_PROB,
                                             pt[0][:, w, :, :].rearrange("p t n -> p (t n)"),
                                             ALU.mult, ALU.subtract).then_inc(lo_ready, 1)
                if valid(k - 2):
                    rows_out(k - 2, u)
                if valid(k):
                    eng.wait_ge(p_ready, k + 1)
                    eng.wait_ge(edge_ready, k + 1)
                    eng.reciprocal(inv[:, u:u + 1], den[:, u:u + 1]).then_inc(inv_ready, 1)
                    eng.wait_ge(inv_ready, k + 1)
                    at_least(eng, rows_ready, k - 1)
                    eng.tensor_tensor(factor[:, u:u + 1], inv[:, u:u + 1], some_edge[:, u:u + 1],
                                      ALU.mult).then_inc(factor_ready, 1)

            def rows_out(k, u):
                eng.wait_ge(out_done, k + 1)
                eng.wait_ge(factor_ready, k + 1)
                head, _ = head_tile(k)
                if turned:
                    at_least(eng, rows_turned, k - 1)
                    eng.scalar_tensor_tensor(rows[:, u, :], op[:, u, 0:P], factor[:, u:u + 1],
                                             bias_all[:, ds(head * P, P)], ALU.mult, ALU.add)\
                       .then_inc(rows_ready, 1)
                else:
                    if isinstance(k, int):
                        eng.wait_ge(in_x[u], 16 * (k // 2 + 1))
                    else:
                        eng.wait_ge(in_x[u], 16 * ((k - u) // 2 + 1))
                    if not isinstance(k, int) or k >= 2:
                        eng.wait_ge(saved[u], 16 * ((k - u) // 2))
                    eng.tensor_tensor(rows[:, u, :], xs[:, u, :], bias_all[:, :], ALU.add)\
                       .then_inc(sum_ready, 1)
                    eng.wait_ge(sum_ready, k + 1)
                    half = D // 2
                    eng.scalar_tensor_tensor(rows[:, u, :].rearrange("p (c n) -> p c n", c=2),
                                             op[:, :, 0:half], factor[:, u:u + 1],
                                             rows[:, u, :].rearrange("p (c n) -> p c n", c=2),
                                             ALU.mult, ALU.add).then_inc(rows_ready, 1)

            run(eng, step)

        @block.tensor
        def _(eng):
            def step(k, u):
                w = (u + 1) % 2
                if valid(k):
                    eng.wait_ge(p_ready, k + 1)
                    at_least(eng, lo_ready, k - 1)
                    for t in range(NT):
                        mm = eng.transpose(tp[:, u, t * P:(t + 1) * P], q[:, u, t * P:(t + 1) * P],
                                           const["ident"][:, :])
                    mm.then_inc(pt_turned, 1)
                if turned and valid(k - 2):
                    eng.wait_ge(rows_ready, k - 1)
                    eng.transpose(op[:, u, P:2 * P], rows[:, u, :], const["ident"][:, :])\
                       .then_inc(rows_turned, 1)
                if valid(k - 1):
                    head, _ = head_tile(k - 1)
                    eng.wait_ge(lo_ready, k)
                    at_least(eng, tl_ready if turned else rows_ready, k - 2 if turned else k - 1)
                    for t in range(NT):
                        for g in range(2 if not turned else 1):
                            cols = min(width, D // 2)
                            place = op[:, g if not turned else w, 0:cols]
                            at = head * P if turned else g * cols
                            mm = split_product(eng, place, [x[:, w, t, :] for x in pt],
                                               [x[:, t, ds(at, cols)] for x in h],
                                               t == 0, t == NT - 1)
                    mm.then_inc(out_done, 1)
            run(eng, step)



def second_products(nc, mem, sem, const, h1t, w2t, att2, z, nad, a_rows):
    G = D // 2
    wf = mem("wf", [P, KC, D], F32)
    wt = [mem(f"wt_{q}", [P, KC, D], F16) for q in ("hi", "lo")]
    att = mem("att", [P, 2, D], F32)
    junk = mem("junk", [P, 2, G], F32)
    a = mem("a", [P, 2, NT], F32)
    a_turned = mem("a_turned", [NT, P], F32)
    PARTS = 4
    in_wt, in_att = [sem(f"sp_in_wt{n}") for n in range(PARTS)], sem("sp_in_att")
    wt_hi, wt_lo, z_done, z_hi, z_lo = (
        sem("sp_wt_hi"), sem("sp_wt_lo"), sem("sp_z"), sem("sp_z_hi"), sem("sp_z_lo"))
    a_read, nad_ready = sem("sp_a_read"), sem("sp_nad")
    at_done, at_read, stored = sem("sp_at"), sem("sp_at_read"), sem("sp_stored")
    with (
        nc.psum_tensor("sp_z", [P, 2, 2 * BANK], F32) as zp,
        nc.psum_tensor("sp_t", [P, BANK], F32) as tp,
        nc.Block() as block,
    ):
        def banks(u):
            return zp[:, u, :].rearrange("p (c n) -> p c n", c=2)[:, :, 0:G]

        def pairs(x, t):
            return x[:, ds(t, 1), :].rearrange("p a (c n) -> p (a c) n", c=2)

        @block.sync
        def _(eng):
            for n in range(PARTS):
                part = slice(n * KC // PARTS, (n + 1) * KC // PARTS)
                eng.dma_start(wf[:, part, :], w2t.rearrange("(k p) c -> p k c", p=P)[:, part, :])\
                   .then_inc(in_wt[n], 16)
            eng.dma_start(att[:, :, :], att2.unsqueeze(0).to_broadcast([P, 2, D])).then_inc(in_att, 16)
            eng.wait_ge(at_read, 1)
            eng.dma_start(a_rows, a_turned[:, :]).then_inc(stored, 16)
            eng.wait_ge(stored, 16)

        @block.tensor
        def _(eng):
            def tile(t, u):
                at_least(eng, a_read, 2 * t - 2)
                for k in range(KC):
                    if isinstance(t, int) and t == 0:
                        eng.wait_ge(wt_lo, k + 1)
                    for c in range(2):
                        last = split_product(eng, zp[:, u, c * BANK:c * BANK + G],
                                             [q[:, k, ds(t * P, P)] for q in h1t],
                                             [q[:, k, c * G:(c + 1) * G] for q in wt],
                                             k == 0, k == KC - 1)
                last.then_inc(z_done, 1)

            rolled(eng, tile, 0, 2, NT, NT)
            eng.wait_ge(a_read, 2 * NT)
            eng.transpose(tp[0:NT, 0:P], a[:, 0, :], const["ident"][:, :]).then_inc(at_done, 1)

        @block.scalar
        def _(eng):
            for k in range(KC):
                eng.wait_ge(in_wt[k * PARTS // KC], 16)
                eng.activation(wt[0][:, k, :], wf[:, k, :], ACT.Copy, scale=S_WEIGHT).then_inc(wt_hi, 1)
            with eng.Fori(0, NT // 2) as pair:
                for u in range(2):
                    t = 2 * pair + u
                    eng.wait_ge(z_done, t + 1)
                    eng.activation(pairs(z[0], t), banks(u), ACT.Copy, scale=1.0 / S_WEIGHT)\
                       .then_inc(z_hi, 1)
            eng.wait_ge(at_done, 1)
            eng.activation(a_turned[:, :], tp[0:NT, 0:P], ACT.Copy).then_inc(at_read, 1)

        @block.vector
        def _(eng):
            for k in range(KC):
                eng.wait_ge(wt_hi, k + 1)
                eng.scalar_tensor_tensor(wt[1][:, k, :], wf[:, k, :], S_WEIGHT, wt[0][:, k, :],
                                         ALU.mult, ALU.subtract).then_inc(wt_lo, 1)
            eng.wait_ge(in_att, 16)
            un = 1.0 / (S_ACT * S_WEIGHT)

            def tile(t, u):
                eng.wait_ge(z_hi, t + 1)
                eng.scalar_tensor_tensor(pairs(z[1], t), banks(u), 1.0 / S_WEIGHT, pairs(z[0], t),
                                         ALU.mult, ALU.subtract).then_inc(z_lo, 1)
                for n in range(2):
                    at_least(eng, a_read, 2 * t + n)
                    eng.tensor_tensor_reduce(junk[:, :, :], banks(u),
                                             att[:, n, :].rearrange("p (c m) -> p c m", c=2),
                                             un, 0.0, ALU.mult, ALU.add,
                                             a[:, n, t:t + 1]).then_inc(a_read, 1)

            for t in range(NT):
                tile(t, t % 2)
            eng.wait_ge(a_read, 2 * NT)
            eng.tensor_scalar(nad[:, :], a[:, 1, :], -0.8, None, ALU.mult).then_inc(nad_ready, 1)
            eng.wait_ge(nad_ready, 1)
            eng.wait_ge(z_lo, NT)


def expert_inputs(nc, mem, sem, x2t, wf, in_w, xw):
    W = EXPERTS * HID
    wt = [mem(f"wt_{q}", [P, KD, W], F16) for q in ("hi", "lo")]
    wt_hi, wt_lo, done, hi_ready, lo_ready = (
        sem("ei_wt_hi"), sem("ei_wt_lo"), sem("ei_done"), sem("ei_hi"), sem("ei_lo"))
    scale = S_ACT / (S_NORM * S_WEIGHT)
    with nc.psum_tensor("ei_ps", [P, 2, W], F32) as ps, nc.Block() as block:

        @block.tensor
        def _(eng):
            def tile(t, u):
                at_least(eng, lo_ready, t - 1)
                for k in range(KD):
                    if isinstance(t, int) and t == 0:
                        eng.wait_ge(wt_lo, k + 1)
                    for c in range(W // BANK):
                        cols = slice(c * BANK, (c + 1) * BANK)
                        last = split_product(eng, ps[:, u, cols],
                                             [q[:, k, ds(t * P, P)] for q in x2t],
                                             [q[:, k, cols] for q in wt], k == 0, k == KD - 1)
                last.then_inc(done, 1)

            rolled(eng, tile, 0, 2, NT, NT)

        @block.scalar
        def _(eng):
            for k in range(KD):
                eng.wait_ge(in_w[k], 16)
                eng.activation(wt[0][:, k, :], wf[:, k, :], ACT.Copy, scale=S_WEIGHT).then_inc(wt_hi, 1)
            with eng.Fori(0, NT // 2) as pair:
                for u in range(2):
                    t = 2 * pair + u
                    eng.wait_ge(done, t + 1)
                    eng.activation(xw[0][:, ds(t, 1), :], ps[:, u, :], ACT.Copy, scale=scale)\
                       .then_inc(hi_ready, 1)

        @block.vector
        def _(eng):
            for k in range(KD):
                eng.wait_ge(wt_hi, k + 1)
                eng.scalar_tensor_tensor(wt[1][:, k, :], wf[:, k, :], S_WEIGHT, wt[0][:, k, :],
                                         ALU.mult, ALU.subtract).then_inc(wt_lo, 1)
            with eng.Fori(0, NT // 2) as pair:
                for u in range(2):
                    t = 2 * pair + u
                    eng.wait_ge(hi_ready, t + 1)
                    eng.scalar_tensor_tensor(xw[1][:, ds(t, 1), :], ps[:, u, :], scale,
                                             xw[0][:, ds(t, 1), :], ALU.mult, ALU.subtract)\
                       .then_inc(lo_ready, 1)


def dispatch(nc, mem, sem, const, x2t, xw, phi, fb1, running_max, hid, logits):
    phf = mem("phf", [P, 2, KD, P], F32)
    ph = [mem(f"ph_{q}", [P, 2, KD, P], F16) for q in ("hi", "lo")]
    lg = mem("lg", [P, 2, N], F32)
    p = mem("p", [P, 2, NP], F32)
    pt = [mem(f"pt_{q}", [P, NT, P], F16) for q in ("hi", "lo")]
    bias = mem("bias", [P, EXPERTS * HID], F32)
    neg = mem("neg", [P, 2], F32)
    den = mem("den", [P, 4], F32)
    inv = mem("inv", [P, 2], F32)
    g, g1, g2, th = (mem(n, [P, HID], F32) for n in ("g", "g1", "g2", "th"))
    in_phi = [sem(f"di_in{i}") for i in range(2)]
    kept = [sem(f"di_kept{i}") for i in range(2)]
    in_bias, zeroed, max_set, max_ready = (
        sem("di_in_bias"), sem("di_zeroed"), sem("di_max_set"), sem("di_max"))
    ph_hi, ph_lo, l_done, lg_ready = sem("di_ph_hi"), sem("di_ph_lo"), sem("di_l"), sem("di_lg")
    top_ready, neg_ready, p_ready, turned_ready = (
        sem("di_top"), sem("di_neg"), sem("di_p"), sem("di_turned"))
    pt_hi, pt_lo, h_done, inv_ready, gel, th_ready = (
        sem("di_pt_hi"), sem("di_pt_lo"), sem("di_h"), sem("di_inv"), sem("di_gelu"), sem("di_th"))
    twice, hid_hi, hid_lo = sem("di_twice"), sem("di_hid_hi"), sem("di_hid_lo")
    top = mem("top", [P, 2], F32)

    with (
        nc.psum_tensor("di_l", [P, 3 * BANK], F32) as lp,
        nc.psum_tensor("di_t", [P, 3 * BANK], F32) as tp,
        nc.psum_tensor("di_h", [P, 2, BANK], F32) as hp,
        nc.Block() as block,
    ):

        def valid(s):
            return not isinstance(s, int) or 0 <= s < ST

        def run(eng, step):
            rolled(eng, step, -1, 3, ST - 1, ST + 2)

        @block.sync
        def _(eng):
            eng.dma_start(bias[:, :], fb1.to_broadcast([P, EXPERTS * HID])).then_inc(in_bias, 16)

            def step(s, u):
                w = (u + 1) % 2
                if valid(s + 1):
                    at_least(eng, ph_lo, s)
                    eng.dma_start(phf[:, w, :, :], phi[ds(s + 1, 1), :, :, :]).then_inc(in_phi[w], 16)
                if valid(s):
                    eng.wait_ge(lg_ready, s + 1)
                    eng.dma_start(logits[ds(s, 1), :, :], lg[:, u, :]).then_inc(kept[u], 16)

            run(eng, step)
            for u in range(2):
                eng.wait_ge(kept[u], 16 * (ST // 2))

        @block.gpsimd
        def _(eng):
            for u in range(2):
                eng.memset(p[:, u, N:NP], 0.0).then_inc(zeroed, 1)
            eng.memset(running_max[:, :], -3e38).then_inc(max_set, 1)
            eng.wait_ge(max_set, 1)

            eng.wait_ge(zeroed, 2)

        @block.scalar
        def _(eng):
            def step(s, u):
                w = (u + 1) % 2
                if valid(s - 1):
                    eng.wait_ge(turned_ready, s)
                    at_least(eng, h_done, s - 1)
                    eng.activation(pt[0][:, :, :].rearrange("p t n -> p (t n)"), tp[:, 0:NP],
                                   ACT.Copy, scale=S_PROB).then_inc(pt_hi, 1)
                if valid(s + 1):
                    eng.wait_ge(in_phi[w], 16 * ((s + 1 - w) // 2 + 1))
                    at_least(eng, l_done, s)
                    eng.activation(ph[0][:, w, :, :], phf[:, w, :, :], ACT.Copy, scale=S_WEIGHT)\
                       .then_inc(ph_hi, 1)
                if valid(s - 2):
                    eng.wait_ge(gel, 4 * (s - 1))
                    at_least(eng, hid_hi, s - 2)
                    eng.activation(th[:, :], g2[:, :], ACT.Tanh, scale=0.7978845608028654)\
                       .then_inc(th_ready, 1)
                if valid(s - 2):
                    eng.wait_ge(twice, s - 1)
                    eng.activation(hid[0][:, ds(s - 2, 1), :], g1[:, :], ACT.Copy, scale=S_ACT / 2)\
                       .then_inc(hid_hi, 1)
                if valid(s):
                    eng.wait_ge(l_done, s + 1)
                    at_least(eng, max_ready, s - 1)
                    at_least(eng, top_ready, s - 1)
                    at_least(eng, p_ready, s - 1)
                    at_least(eng, kept[u], 16 * ((s - u) // 2))
                    eng.activation(lg[:, u, :], lp[:, 0:N], ACT.Copy, scale=1.0 / (S_NORM * S_WEIGHT))\
                       .then_inc(lg_ready, 1)
                if valid(s):
                    eng.wait_ge(neg_ready, s + 1)
                    at_least(eng, turned_ready, s - 1)
                    at_least(eng, inv_ready, 2 * (s - 1))
                    eng.activation(p[:, u, 0:N], lg[:, u, :], ACT.Exp, bias=neg[:, u:u + 1],
                                   accum_out=den[:, u:u + 1]).then_inc(p_ready, 1)
            run(eng, step)

        @block.vector
        def _(eng):
            eng.wait_ge(in_bias, 16)
            eng.wait_ge(max_set, 1)

            def step(s, u):
                w = (u + 1) % 2
                if valid(s - 1):
                    eng.wait_ge(pt_hi, s)
                    eng.scalar_tensor_tensor(pt[1][:, :, :].rearrange("p t n -> p (t n)"), tp[:, 0:NP],
                                             S_PROB, pt[0][:, :, :].rearrange("p t n -> p (t n)"),
                                             ALU.mult, ALU.subtract).then_inc(pt_lo, 1)
                if valid(s + 1):
                    eng.wait_ge(ph_hi, s + 2)
                    eng.scalar_tensor_tensor(ph[1][:, w, :, :].rearrange("p k n -> p (k n)"),
                                             phf[:, w, :, :].rearrange("p k n -> p (k n)"), S_WEIGHT,
                                             ph[0][:, w, :, :].rearrange("p k n -> p (k n)"),
                                             ALU.mult, ALU.subtract).then_inc(ph_lo, 1)
                if valid(s - 2):
                    k = s - 2
                    expert = k // STE
                    eng.wait_ge(h_done, k + 1)
                    at_least(eng, hid_lo, k)
                    eng.scalar_tensor_tensor(g[:, :], hp[:, u, 0:HID], inv[:, u:u + 1],
                                             bias[:, ds(expert * HID, HID)], ALU.mult, ALU.add)\
                       .then_inc(gel, 1)
                    eng.wait_ge(gel, 4 * k + 1)
                    eng.tensor_tensor(g1[:, :], g[:, :], g[:, :], ALU.mult).then_inc(gel, 1)
                    eng.wait_ge(gel, 4 * k + 2)
                    eng.tensor_scalar(g1[:, :], g1[:, :], 0.044715, 1.0, ALU.mult, ALU.add)\
                       .then_inc(gel, 1)
                    eng.wait_ge(gel, 4 * k + 3)
                    eng.tensor_tensor(g2[:, :], g1[:, :], g[:, :], ALU.mult).then_inc(gel, 1)
                if valid(s - 2):
                    k = s - 2
                    eng.wait_ge(th_ready, k + 1)
                    eng.scalar_tensor_tensor(g1[:, :], th[:, :], 1.0, g[:, :], ALU.add, ALU.mult)\
                       .then_inc(twice, 1)
                    eng.wait_ge(hid_hi, k + 1)
                    eng.scalar_tensor_tensor(hid[1][:, ds(k, 1), :], g1[:, :], S_ACT / 2,
                                             hid[0][:, ds(k, 1), :], ALU.mult, ALU.subtract)\
                       .then_inc(hid_lo, 1)
                if valid(s):
                    eng.wait_ge(lg_ready, s + 1)
                    at_least(eng, neg_ready, s - 1)
                    eng.tensor_reduce(top[:, u:u + 1], lg[:, u, :], AX_X, ALU.max).then_inc(top_ready, 1)
                    eng.wait_ge(top_ready, s + 1)
                    at_least(eng, p_ready, s - 1)
                    eng.tensor_scalar(neg[:, u:u + 1], top[:, u:u + 1], -1.0, None, ALU.mult)\
                       .then_inc(neg_ready, 1)
                    at_least(eng, max_ready, s)
                    eng.tensor_tensor(running_max[:, 0:N], running_max[:, 0:N], lg[:, u, :],
                                      ALU.max).then_inc(max_ready, 1)
                if valid(s):
                    eng.wait_ge(p_ready, s + 1)
                    at_least(eng, gel, 4 * (s - 1))
                    eng.reciprocal(inv[:, u:u + 1], den[:, u:u + 1]).then_inc(inv_ready, 1)
                    eng.wait_ge(inv_ready, 2 * s + 1)
                    eng.tensor_scalar(inv[:, u:u + 1], inv[:, u:u + 1], 1.0 / (S_PROB * S_ACT), None,
                                      ALU.mult).then_inc(inv_ready, 1)
            run(eng, step)
            eng.wait_ge(max_ready, ST)
            eng.wait_ge(hid_lo, ST)

        @block.tensor
        def _(eng):
            eng.wait_ge(zeroed, 2)

            def step(s, u):
                w = (u + 1) % 2
                def logits_of(channels):
                    for k in channels:
                        for a, n in CHUNKS:
                            mm = split_product(eng, lp[:, a:a + n], [q[:, u, k, :] for q in ph],
                                               [q[:, k, a:a + n] for q in x2t],
                                               k == 0, k == KD - 1)
                    return mm

                if valid(s):
                    eng.wait_ge(ph_lo, s + 1)
                    at_least(eng, lg_ready, s)
                    logits_of(range(KD // 2))
                if valid(s - 1):
                    eng.wait_ge(p_ready, s)
                    at_least(eng, pt_lo, s - 1)
                    for t in range(NT):
                        mm = eng.transpose(tp[:, t * P:(t + 1) * P], p[:, w, t * P:(t + 1) * P],
                                           const["ident"][:, :])
                    mm.then_inc(turned_ready, 1)
                if valid(s):
                    logits_of(range(KD // 2, KD)).then_inc(l_done, 1)
                if valid(s - 1):
                    expert = (s - 1) // STE
                    eng.wait_ge(pt_lo, s)
                    at_least(eng, gel, 4 * (s - 3) + 1)
                    for t in range(NT):
                        mm = split_product(eng, hp[:, w, 0:HID], [q[:, t, :] for q in pt],
                                           [q[:, t, ds(expert * HID, HID)] for q in xw],
                                           t == 0, t == NT - 1)
                    mm.then_inc(h_done, 1)
            run(eng, step)


def combine(nc, mem, sem, const, running_max, hid, comb, slot_sums, lt, max_rows, logits):
    STEPS = STE // 2
    GROUPS = 2 * EXPERTS
    COLS = ((0, 320), (320, HALF - 320))
    top = mem("top", [P, NP], F32)
    top_col = mem("top_col", [P, NT], F32)
    top_row = mem("top_row", [NT, P], F32)
    p = mem("p", [P, 2, 2, HALF], F32)
    ps = [mem(f"ps_{q}", [P, 2, 2, HALF], F16) for q in ("hi", "lo")]
    sums = mem("sums", [P, 2, 2, HALF], F32)
    sum_row = mem("sum_row", [1, 2, HALF], F32)
    sums_dram = nc.dram_tensor("slot_sums", [EXPERTS, N], F32).ap()
    max_turned, max_col, max_turned2, max_row, row_kept, in_top = (
        sem("co_mt"), sem("co_mc"), sem("co_mt2"), sem("co_mr"), sem("co_kept"), sem("co_top"))
    in_l = [sem(f"co_in{i}") for i in range(STEPS)]
    sub_ready, p_ready, hi_ready, lo_ready, sum_ready = (
        sem("co_sub"), sem("co_p"), sem("co_hi"), sem("co_lo"), sem("co_sum"))
    used, rows_done, row_read = sem("co_used"), sem("co_rows"), sem("co_row_read")
    c_hi, c_lo, pads, sums_in = sem("co_chi"), sem("co_clo"), sem("co_pads"), sem("co_sums_in")
    sums_kept = [sem(f"co_sums_kept{i}") for i in range(2)]
    unscale = S_COMB / (S_PROB * S_ACT)
    BLOCKS = [(ht, c) for ht in range(KH) for c in range(2)]

    def groups(eng, steps, finish):
        def one(G, v, more):
            for i in range(1, STEPS):
                steps(G, v, i)
            if more:
                steps(G + 1, 1 - v, 0)
            finish(G, v)

        steps(0, 0, 0)
        one(0, 0, True)
        one(1, 1, True)
        with eng.Fori(1, GROUPS // 2 - 1) as pair:
            one(2 * pair, 0, True)
            one(2 * pair + 1, 1, True)
        one(GROUPS - 2, 0, True)
        one(GROUPS - 1, 1, False)

    with (
        nc.psum_tensor("co_c", [P, len(BLOCKS), BANK], F32) as cp,
        nc.psum_tensor("co_s", [P, 2, BANK], F32) as sp,
        nc.Block() as block,
    ):

        def turned_max(t):
            return cp[:, t // 4, (t % 4) * P:(t % 4 + 1) * P]

        @block.sync
        def _(eng):
            def load(G, v, i):
                at_least(eng, sub_ready, STEPS * (G - 1) + i + 1)
                half, expert = G // EXPERTS, G % EXPERTS
                eng.dma_start(lt[:, i, :, :],
                              logits[ds(expert * STE + 2 * i, 2), :, ds(half * HALF, HALF)]
                              .rearrange("s p n -> p s n")).then_inc(in_l[i], 16)

            eng.wait_ge(max_row, 1)
            eng.dma_start(max_rows, top_row[:, :]).then_inc(row_kept, 16)
            eng.wait_ge(row_kept, 16)
            eng.dma_start(top[:, :].rearrange("p (t n) -> p t n", t=NT),
                          max_rows.unsqueeze(0).to_broadcast([P, NT, P])).then_inc(in_top, 16)
            groups(eng, load, lambda G, v: None)
            for q in sums_kept:
                eng.wait_ge(q, 16 * (GROUPS // 2))
            eng.wait_ge(pads, 3)
            eng.dma_start(slot_sums[:, 0:N], sums_dram).then_inc(sums_in, 16)
            eng.wait_ge(sums_in, 16)

        @block.gpsimd
        def _(eng):
            for q in comb:
                eng.memset(q[:, :, N:NP], 0.0).then_inc(pads, 1)
            eng.memset(slot_sums[:, :], 1.0).then_inc(pads, 1)
            eng.wait_ge(pads, 3)

            def step(G, v, i):
                k = STEPS * G + i
                if i == 0:
                    return
                if i == 1:
                    at_least(eng, rows_done, G - 1)
                eng.wait_ge(p_ready, k + 1)
                at_least(eng, sum_ready, (STEPS - 1) * G + i - 1)
                eng.tensor_tensor(sums[:, v, :, :], p[:, 0, :, :] if i == 1 else sums[:, v, :, :],
                                  p[:, i % 2, :, :], ALU.add).then_inc(sum_ready, 1)

            groups(eng, step, lambda G, v: None)

        @block.scalar
        def _(eng):
            eng.wait_ge(max_turned2, 1)
            eng.activation(top_row[:, :], sp[0:NT, 0, 0:P], ACT.Copy).then_inc(max_row, 1)

            def step(G, v, i):
                k = STEPS * G + i
                u = i % 2
                eng.wait_ge(sub_ready, k + 1)
                eng.activation(p[:, u, :, :], p[:, u, :, :], ACT.Exp).then_inc(p_ready, 1)
                eng.wait_ge(p_ready, k + 1)
                at_least(eng, used, k - 1)
                eng.activation(ps[0][:, u, :, :], p[:, u, :, :], ACT.Copy, scale=S_PROB)\
                   .then_inc(hi_ready, 1)

            def finish(G, v):
                half, expert = G // EXPERTS, G % EXPERTS
                eng.wait_ge(used, STEPS * (G + 1))
                for n, (ht, c) in enumerate(BLOCKS):
                    a, w = COLS[c]
                    eng.activation(comb[0][:, ds(expert * KH + ht, 1), ds(half * HALF + a, w)],
                                   cp[:, n, 0:w], ACT.Copy, scale=unscale).then_inc(c_hi, 1)
                eng.wait_ge(rows_done, G + 1)
                at_least(eng, sums_kept[v], 8 * (G - v))
                for c, (a, w) in enumerate(COLS):
                    eng.activation(sum_row[:, v, a:a + w], sp[0:1, c, 0:w], ACT.Copy, scale=S_COMB)\
                       .then_inc(row_read, 1)
                eng.wait_ge(row_read, 2 * G + 2)
                eng.dma_start(sums_dram[ds(expert, 1), ds(half * HALF, HALF)], sum_row[:, v, :])\
                   .then_inc(sums_kept[v], 16)

            groups(eng, step, finish)

        @block.vector
        def _(eng):
            eng.wait_ge(max_turned, 1)
            for t in range(NT):
                eng.tensor_reduce(top_col[:, t:t + 1], turned_max(t), AX_X, ALU.max).then_inc(max_col, 1)
            eng.wait_ge(in_top, 16)

            def subtract(G, i):
                k = STEPS * G + i
                half = G // EXPERTS
                u = i % 2
                eng.wait_ge(in_l[i], 16 * (G + 1))
                at_least(eng, sum_ready, (STEPS - 1) * G + (i - 1 if i < 2 else 1 if i == 2 else i - 2))
                at_least(eng, lo_ready, k - 1)
                eng.tensor_tensor(p[:, u, :, :], lt[:, i, :, :],
                                  top[:, ds(half * HALF, HALF)].unsqueeze(1)
                                  .to_broadcast([P, 2, HALF]), ALU.subtract).then_inc(sub_ready, 1)

            def step(G, v, i):
                k = STEPS * G + i
                u = i % 2
                if i < STEPS - 1 and i != 1:
                    subtract(G, i + 1)
                elif i == STEPS - 1 and not (isinstance(G, int) and G + 1 == GROUPS):
                    subtract(G + 1, 0)
                eng.wait_ge(hi_ready, k + 1)
                eng.scalar_tensor_tensor(ps[1][:, u, :, :], p[:, u, :, :], S_PROB, ps[0][:, u, :, :],
                                         ALU.mult, ALU.subtract).then_inc(lo_ready, 1)
                if i == 1:
                    subtract(G, 2)

            def finish(G, v):
                half, expert = G // EXPERTS, G % EXPERTS
                for n, (ht, c) in enumerate(BLOCKS):
                    a, w = COLS[c]
                    eng.wait_ge(c_hi, len(BLOCKS) * G + n + 1)
                    place = (slice(None), ds(expert * KH + ht, 1), ds(half * HALF + a, w))
                    eng.scalar_tensor_tensor(comb[1][place], cp[:, n, 0:w], unscale, comb[0][place],
                                             ALU.mult, ALU.subtract).then_inc(c_lo, 1)

            subtract(0, 0)
            groups(eng, step, finish)

        @block.tensor
        def _(eng):
            for t in range(NT):
                mm = eng.transpose(turned_max(t), running_max[:, t * P:(t + 1) * P],
                                   const["ident"][:, :])
            mm.then_inc(max_turned, 1)
            eng.wait_ge(max_col, NT)
            eng.transpose(sp[0:NT, 0, 0:P], top_col[:, :], const["ident"][:, :]).then_inc(max_turned2, 1)
            eng.wait_ge(max_row, 1)

            def group(G, v):
                expert = G % EXPERTS
                for i in range(STEPS):
                    k = STEPS * G + i
                    eng.wait_ge(lo_ready, k + 1)
                    for n, (ht, c) in enumerate(BLOCKS):
                        a, w = COLS[c]
                        if i == 0:
                            at_least(eng, c_lo, len(BLOCKS) * (G - 1) + n + 1)
                        for s in range(2):
                            mm = split_product(
                                eng, cp[:, n, 0:w],
                                [q[:, ds(expert * STE + 2 * i + s, 1), ht * P:(ht + 1) * P] for q in hid],
                                [q[:, i % 2, s, a:a + w] for q in ps],
                                i == 0 and s == 0, i == STEPS - 1 and s == 1)
                    mm.then_inc(used, 1)
                eng.wait_ge(sum_ready, (STEPS - 1) * (G + 1))
                at_least(eng, row_read, 2 * G)
                for c, (a, w) in enumerate(COLS):
                    for s in range(2):
                        mm = eng.matmul(sp[0:1, c, 0:w], const["one"][:, :], sums[:, v, s, a:a + w],
                                        start=s == 0, stop=s == 1)
                mm.then_inc(rows_done, 1)

            group(0, 0)
            group(1, 1)
            with eng.Fori(1, GROUPS // 2) as pair:
                group(2 * pair, 0)
                group(2 * pair + 1, 1)


def expert_outputs(nc, mem, sem, comb, slot_sums, wf, wt, fw2, fb2, x1, out):
    K = EXPERTS * KH
    G = D // 2
    bf = mem("bf", [EXPERTS, D], F32)
    bt = [mem(f"bt_{q}", [EXPERTS, D], F16) for q in ("hi", "lo")]
    st = [mem(f"st_{q}", [EXPERTS, NP], F16) for q in ("hi", "lo")]
    ones = mem("ones", [EXPERTS, 2], F16)
    xs = mem("xs", [P, 2, D], F32)
    y = mem("y", [P, 2, D], F32)
    inv = mem("inv", [P, 2], F32)
    in_b, in_w = sem("eo_in_b"), [sem(f"eo_in_w{k}") for k in range(K)]
    in_x, kept = [sem(f"eo_in_x{i}") for i in range(2)], [sem(f"eo_kept{i}") for i in range(2)]
    ones_ready, small_hi, small_lo, wt_hi, wt_lo = (
        sem("eo_ones"), sem("eo_small_hi"), sem("eo_small_lo"), sem("eo_wt_hi"), sem("eo_wt_lo"))
    done, inv_ready, y_ready = sem("eo_done"), sem("eo_inv"), sem("eo_y")
    with (
        nc.psum_tensor("eo_y", [P, 2, 2 * BANK], F32) as yp,
        nc.psum_tensor("eo_r", [P, 2, BANK], F32) as rp,
        nc.Block() as block,
    ):

        def banks(u):
            return yp[:, u, :].rearrange("p (c n) -> p c n", c=2)[:, :, 0:G]

        def pairs(x, u):
            return x[:, u, :].rearrange("p (c n) -> p c n", c=2)

        def store(eng, t):
            rows = min(P, N - t * P)
            eng.wait_ge(y_ready, t + 1)
            eng.dma_start(out[t * P:t * P + rows, :], y[0:rows, t % 2, :]).then_inc(kept[t % 2], 16)

        @block.sync
        def _(eng):
            eng.dma_start(bf[:, :], fb2).then_inc(in_b, 16)
            for k in range(K):
                eng.dma_start(wf[:, k, :], fw2[:, k, :]).then_inc(in_w[k], 16)
            for t in range(NT):
                u = t % 2
                if t >= 2:
                    eng.wait_ge(y_ready, t - 1)
                eng.dma_start(xs[:, u, :], x1[t * P:(t + 1) * P, :]).then_inc(in_x[u], 16)
                if t >= 1:
                    store(eng, t - 1)
            store(eng, NT - 1)
            for u in range(2):
                eng.wait_ge(kept[u], 16 * (NT // 2))

        @block.gpsimd
        def _(eng):
            eng.memset(ones[:, :], 1.0).then_inc(ones_ready, 1)

        @block.scalar
        def _(eng):
            eng.activation(st[0][:, :], slot_sums[:, :], ACT.Copy).then_inc(small_hi, 1)
            eng.wait_ge(in_b, 16)
            eng.activation(bt[0][:, :], bf[:, :], ACT.Copy, scale=S_WEIGHT).then_inc(small_hi, 1)
            for k in range(K):
                eng.wait_ge(in_w[k], 16)
                eng.activation(wt[0][:, k, :], wf[:, k, :], ACT.Copy, scale=S_WEIGHT).then_inc(wt_hi, 1)

        @block.vector
        def _(eng):
            eng.wait_ge(small_hi, 2)
            eng.tensor_tensor(st[1][:, :], slot_sums[:, :], st[0][:, :], ALU.subtract)\
               .then_inc(small_lo, 1)
            eng.scalar_tensor_tensor(bt[1][:, :], bf[:, :], S_WEIGHT, bt[0][:, :], ALU.mult,
                                     ALU.subtract).then_inc(small_lo, 1)
            for k in range(K):
                eng.wait_ge(wt_hi, k + 1)
                eng.scalar_tensor_tensor(wt[1][:, k, :], wf[:, k, :], S_WEIGHT, wt[0][:, k, :],
                                         ALU.mult, ALU.subtract).then_inc(wt_lo, 1)
            for t in range(NT):
                u = t % 2
                eng.wait_ge(done, t + 1)
                eng.reciprocal(inv[:, u:u + 1], rp[:, u, 0:1]).then_inc(inv_ready, 1)
                eng.wait_ge(inv_ready, 2 * t + 1)
                eng.tensor_scalar(inv[:, u:u + 1], inv[:, u:u + 1], 1.0 / S_WEIGHT, None, ALU.mult)\
                   .then_inc(inv_ready, 1)
                eng.wait_ge(inv_ready, 2 * t + 2)
                eng.wait_ge(in_x[u], 16 * (t // 2 + 1))
                if t >= 2:
                    eng.wait_ge(kept[u], 16 * (t // 2))
                eng.scalar_tensor_tensor(pairs(y, u), banks(u), inv[:, u:u + 1], pairs(xs, u),
                                         ALU.mult, ALU.add).then_inc(y_ready, 1)

        @block.tensor
        def _(eng):
            eng.wait_ge(ones_ready, 1)
            eng.wait_ge(small_lo, 2)

            def tile(t, u):
                at_least(eng, y_ready, t - 1)
                for k in range(K):
                    if isinstance(t, int) and t == 0:
                        eng.wait_ge(wt_lo, k + 1)
                    for c in range(2):
                        split_product(eng, yp[:, u, c * BANK:c * BANK + G],
                                      [q[:, k, ds(t * P, P)] for q in comb],
                                      [q[:, k, c * G:(c + 1) * G] for q in wt], k == 0, False)
                for c in range(2):
                    split_product(eng, yp[:, u, c * BANK:c * BANK + G],
                                  [q[:, ds(t * P, P)] for q in st],
                                  [q[:, c * G:(c + 1) * G] for q in bt], False, True)
                for n, q in enumerate(st):
                    last = eng.matmul(rp[:, u, 0:2], q[:, ds(t * P, P)], ones[:, :],
                                      start=n == 0, stop=n == 1)
                last.then_inc(done, 1)

            rolled(eng, tile, 0, 2, NT, NT)


def kernel(**inputs):
    import concourse.bacc as bacc
    from concourse.bass_utils import run_bass_kernel_spmd

    given = {k.removeprefix("L0_"): np.asarray(v) for k, v in inputs.items()}
    x = np.zeros((NP, D), np.float32)
    x[:N] = given["x"]
    edges = np.full((2, ET * P), NO_NODE, np.int32)
    edges[0, :E] = given["src"]
    edges[1, :E] = given["dst"]
    edges = edges.reshape(2, ET, P).transpose(2, 0, 1)
    att1 = np.stack([given["gnn_att_src1"].reshape(-1), given["gnn_att_dst1"].reshape(-1)])
    att2 = np.concatenate([given["gnn_att_src2"], given["gnn_att_dst2"]])
    phi = given["ffn_phi"].reshape(ST, P, KD, P).transpose(0, 3, 2, 1)
    w1 = given["ffn_w1"].reshape(EXPERTS, KD, P, HID).transpose(2, 1, 0, 3).reshape(P, KD, -1)
    w2 = given["ffn_w2"].reshape(EXPERTS * KH, P, D).transpose(1, 0, 2)
    arrays = {
        "x": x, "edges": edges, "w1t": given["gnn_W1"].T, "att1": att1,
        "gb1": given["gnn_b1"].reshape(1, C1), "w2t": given["gnn_W2"].T, "att2": att2,
        "gb2": given["gnn_b2"].reshape(1, D), "phi": phi, "fw1": w1,
        "fb1": given["ffn_b1"].reshape(1, -1), "fw2": w2, "fb2": given["ffn_b2"],
    }
    arrays = {f"in_{k}": np.ascontiguousarray(v) for k, v in arrays.items()}
    nc = bacc.Bacc("TRN2", target_bir_lowering=False, num_devices=1)
    args = [nc.dram_tensor(k, v.shape, mybir.dt.from_np(v.dtype), kind="ExternalInput").ap()
            for k, v in arrays.items()]
    out = nc.dram_tensor("out_x", (N, D), F32, kind="ExternalOutput").ap()
    build(nc, *args, out)
    got = run_bass_kernel_spmd(nc, [arrays], core_ids=[0])
    return got.results[0]["out_x"]
```
